# Optimizing a Trainium2 kernel written in Bass

```python
import numpy as np
import jax
import jax.numpy as jnp

def _softmax(x, axis=-1):
    return jax.nn.softmax(x, axis=axis)

def _gelu(x):
    return jax.nn.gelu(x, approximate=True)

def _silu(x):
    return jax.nn.silu(x)

def _sigmoid(x):
    return jax.nn.sigmoid(x)

def _layernorm(x, axis=-1, eps=1e-05):
    m = jnp.mean(x, axis=axis, keepdims=True)
    v = jnp.var(x, axis=axis, keepdims=True)
    return (x - m) / jnp.sqrt(v + eps)

def _scatter_add(tgt, idx, src, axis=0):
    return tgt.at[idx].add(src)

def _segment_sum(src, seg, n):
    return jax.ops.segment_sum(src, seg, n)
kernel_name = 'mk_xattn_ffn_d1_seqx_r4_d82c39'

def setup_inputs(seed: int=0):
    np.random.seed(seed)
    _w = jnp.asarray

    def _rec_inputs():
        import jax
        import jax.numpy as jnp
        _rk = jax.random.key(seed)
        x = 7.22e-05 + 1 * jax.random.normal(jax.random.fold_in(_rk, 1), (2, 1024, 256), jnp.float32)
        _lenS = 1024 - jax.random.randint(jax.random.fold_in(_rk, 7), (2,), 0, max(1, 1024 // 4) + 1, jnp.int32)
        _lenS2 = 77 - jax.random.randint(jax.random.fold_in(_rk, 8), (2,), 0, max(1, 77 // 4) + 1, jnp.int32)
        _ctx_1024P = jax.random.normal(jax.random.fold_in(_rk, 11), (2, 16, 256), jnp.float32)
        _ctx_1024c = jax.random.dirichlet(jax.random.fold_in(_rk, 511), 0.3 * jnp.ones((16,), jnp.float32), (2, 77))
        _ctx_1024t = jnp.einsum('bsk,bkd->bsd', _ctx_1024c, _ctx_1024P)
        _ctx_1024t = _ctx_1024t * jax.lax.rsqrt(jnp.mean(jnp.square(_ctx_1024t)) + 1e-12) * 0.953939
        ctx_1024 = 4.13588e-05 + 0.999923 * (_ctx_1024t + 0.3 * jax.random.normal(jax.random.fold_in(_rk, 611), (2, 77, 256), jnp.float32))
        return (x, ctx_1024, _lenS2)
    x, ctx_1024, _lenS2 = _rec_inputs()

    def _L0_xattn_setup():
        import jax, jax.numpy as jnp
        import numpy as np
        B, N, D, H = (4, 512, 256, 16)
        DH = D // H
        key = jax.random.key(seed)
        ks = jax.random.split(key, 8)
        scale = 1.0 / np.sqrt(D)
        return {'Q': jax.random.normal(ks[0], (B, N, D), dtype=jnp.float32), 'K': jax.random.normal(ks[1], (B, N, D), dtype=jnp.float32), 'V': jax.random.normal(ks[2], (B, N, D), dtype=jnp.float32), 'valid_lens': jax.random.randint(ks[3], (B,), 1, N, dtype=jnp.int32), 'Wq': jax.random.normal(ks[4], (D, D), dtype=jnp.float32) * scale, 'Wk': jax.random.normal(ks[5], (D, D), dtype=jnp.float32) * scale, 'Wv': jax.random.normal(ks[6], (D, D), dtype=jnp.float32) * scale, 'Wo': jax.random.normal(ks[7], (D, D), dtype=jnp.float32) * scale}
    _L0_xattn_all = _L0_xattn_setup()
    _L0_xattn_in = {k: v for k, v in _L0_xattn_all.items() if k in ('Wq', 'Wk', 'Wv', 'Wo')}
    del _L0_xattn_all

    def _L0_ffn_setup():
        import jax, jax.numpy as jnp
        import numpy as np
        TOP_K = 2
        key = jax.random.key(seed)
        ks = jax.random.split(key, 8)
        B, S, D = (2, 512, 256)
        N_r, N_s = (16, 2)
        u = jax.random.normal(ks[0], (B, S, D), dtype=jnp.float32)
        centroids = jax.random.normal(ks[1], (N_r, D), dtype=jnp.float32)
        expert_biases = jnp.zeros((N_r,), dtype=jnp.float32)
        Wr = jax.random.normal(ks[2], (N_r, D, D), dtype=jnp.float32) * (1.0 / np.sqrt(D))
        br = jax.random.normal(ks[3], (N_r, D), dtype=jnp.float32) * 0.01
        Ws = jax.random.normal(ks[4], (N_s, D, D), dtype=jnp.float32) * (1.0 / np.sqrt(D))
        bs = jax.random.normal(ks[5], (N_s, D), dtype=jnp.float32) * 0.01
        return {'u': u, 'centroids': centroids, 'expert_biases': expert_biases, 'Wr': Wr, 'br': br, 'Ws': Ws, 'bs': bs}
    _L0_ffn_all = _L0_ffn_setup()
    _L0_ffn_in = {k: v for k, v in _L0_ffn_all.items() if k in ('centroids', 'expert_biases', 'Wr', 'br', 'Ws', 'bs')}
    del _L0_ffn_all
    return {'x': x, 'ctx_1024': ctx_1024, '_lenS2': _lenS2, 'L0_xattn_Wq': _L0_xattn_in['Wq'], 'L0_xattn_Wk': _L0_xattn_in['Wk'], 'L0_xattn_Wv': _L0_xattn_in['Wv'], 'L0_xattn_Wo': _L0_xattn_in['Wo'], 'L0_ffn_centroids': _L0_ffn_in['centroids'], 'L0_ffn_expert_biases': _L0_ffn_in['expert_biases'], 'L0_ffn_Wr': _L0_ffn_in['Wr'], 'L0_ffn_br': _L0_ffn_in['br'], 'L0_ffn_Ws': _L0_ffn_in['Ws'], 'L0_ffn_bs': _L0_ffn_in['bs']}

def reference(x, ctx_1024, _lenS2, L0_xattn_Wq, L0_xattn_Wk, L0_xattn_Wv, L0_xattn_Wo, L0_ffn_centroids, L0_ffn_expert_biases, L0_ffn_Wr, L0_ffn_br, L0_ffn_Ws, L0_ffn_bs):
    import jax
    import jax.numpy as jnp

    def _L0_xattn_ref(Q, K, V, valid_lens, Wq, Wk, Wv, Wo):
        import jax, jax.numpy as jnp
        import numpy as np
        B, N, D, H = (4, 512, 256, 16)
        DH = D // H
        b, nq, d = Q.shape
        nk = K.shape[1]
        dh = d // H
        q = (Q @ Wq).reshape(b, nq, H, dh).transpose(0, 2, 1, 3)
        k = (K @ Wk).reshape(b, nk, H, dh).transpose(0, 2, 1, 3)
        v = (V @ Wv).reshape(b, nk, H, dh).transpose(0, 2, 1, 3)
        S = jnp.einsum('bhqd,bhkd->bhqk', q, k) / jnp.sqrt(jnp.asarray(dh, (S_dtype := q.dtype)))
        key_pos = jnp.arange(nk)
        mask = key_pos[None, :] < valid_lens[:, None]
        S = jnp.where(mask[:, None, None, :], S, jnp.asarray(-1e+20, S.dtype))
        A = jax.nn.softmax(S, axis=-1)
        O = jnp.einsum('bhqk,bhkd->bhqd', A, v)
        O = O.transpose(0, 2, 1, 3).reshape(b, nq, d)
        return O @ Wo

    def _L0_ffn_ref(u, centroids, expert_biases, Wr, br, Ws, bs):
        import jax, jax.numpy as jnp
        import numpy as np
        TOP_K = 2
        N_r = centroids.shape[0]
        N_s = Ws.shape[0]
        raw_scores = jnp.einsum('bsd,ed->bse', u, centroids)
        s = jax.nn.softmax(raw_scores + expert_biases, axis=-1)
        topk_vals, topk_idx = jax.lax.top_k(s, TOP_K)
        g_topk = jnp.sum(jax.nn.one_hot(topk_idx, N_r, dtype=s.dtype) * topk_vals[..., None], axis=-2)
        xe = jnp.einsum('bsd,eod->bseo', u, Wr) + br
        routed = jnp.einsum('bse,bseo->bso', g_topk, xe)
        shared = (jnp.einsum('bsd,eod->bso', u, Ws) + jnp.sum(bs, axis=0)) / N_s
        return u + routed + shared
    x = x + _L0_xattn_ref(_layernorm(x, axis=-1), ctx_1024, ctx_1024, _lenS2, L0_xattn_Wq, L0_xattn_Wk, L0_xattn_Wv, L0_xattn_Wo)
    x = x + _L0_ffn_ref(_layernorm(x, axis=-1), L0_ffn_centroids, L0_ffn_expert_biases, L0_ffn_Wr, L0_ffn_br, L0_ffn_Ws, L0_ffn_bs)
    return x

_drawn_inputs = setup_inputs


def setup_inputs(seed=0):
    import zlib

    import numpy as np

    out = dict(_drawn_inputs(seed))
    spreads = {'L0_ffn_expert_biases': (0.0, 0.8)}
    factors = {'L0_ffn_br': 8.0, 'L0_ffn_bs': 8.0}
    for name, (base, spread) in spreads.items():
        noise = np.random.default_rng([zlib.crc32(name.encode()), seed]).standard_normal(out[name].shape)
        drawn = base * np.exp(spread * noise) if base else spread * noise
        out[name] = jnp.asarray(drawn.astype(out[name].dtype))
    for name, factor in factors.items():
        out[name] = (out[name] * factor).astype(out[name].dtype)
    return out
```

```python
import numpy as np
from contextlib import ExitStack

import concourse.bass as bass
from concourse import mybir

BATCH, SEQ, D, HEADS, NKEYS = 2, 1024, 256, 16, 77
DH = D // HEADS
EXPERTS, SHARED, TOPK = 16, 2, 2
P = 128
TOKENS = BATCH * SEQ
TILES = TOKENS // P
DC = D // P
HALF = HEADS // 2 * NKEYS
QUART = HALF // 2
ROWS = HEADS * NKEYS
CH = -(-ROWS // P)
LASTROWS = ROWS - (CH - 1) * P
SPAN = 3
HEAD0 = [min(P * c // NKEYS, HEADS - SPAN) for c in range(CH)]
GROUPS = [(0, 4), (4, 8), (8, CH)]
ODIM = DH + 1
EPS = 1e-5

REGION = TOKENS + P
DUMMY = EXPERTS * REGION
ROW = D + 1
YROWS = TOPK * TOKENS
PADROW = YROWS
LISTS = 4 * -(-(YROWS // P + EXPERTS - 1) // 4)

_COLS, _n = {}, 0
for _name, _w in (("ident", P), ("before", P), ("headmask", HEADS // 2), ("key", NKEYS),
                  ("rowkey", CH), ("rowhead", CH * SPAN), ("expert", EXPERTS), ("region", EXPERTS),
                  ("tilerows", EXPERTS), ("upto", EXPERTS * EXPERTS), ("lists", LISTS), ("ids", TILES * TOPK)):
    _COLS[_name] = (_n, _n + _w)
    _n += _w
NCONST = _n


def _constants():
    c = np.zeros((P, NCONST), np.float32)
    p = np.arange(P)

    def put(name, a):
        c[:, slice(*_COLS[name])] = a

    put("ident", np.eye(P))
    put("before", p[:, None] < p[None, :])
    put("headmask", (p[:, None] // DH == np.arange(HEADS // 2)[None, :]) / np.sqrt(DH))
    put("key", np.arange(NKEYS)[None, :])
    row = p[:, None] + P * np.arange(CH)[None, :]
    put("rowkey", row % NKEYS)
    head = np.array(HEAD0)[:, None] + np.arange(SPAN)[None, :]
    put("rowhead", ((row[:, :, None] // NKEYS == head[None]) & (row < ROWS)[:, :, None]).reshape(P, -1))
    put("expert", np.arange(EXPERTS)[None, :])
    put("region", np.arange(EXPERTS)[None, :] * REGION)
    put("tilerows", np.arange(EXPERTS)[None, :] * P)
    e = np.arange(EXPERTS)
    put("upto", (e[None, :] <= e[:, None]).reshape(1, -1))
    put("lists", np.arange(LISTS)[None, :])
    put("ids", (p[:, None, None] + P * np.arange(TILES)[None, :, None]
                + TOKENS * np.arange(TOPK)[None, None, :]).reshape(P, -1))
    return c


def build(nc, x_in, ctxT_in, lens_in, wq_in, wk_in, wv_in, wo_in, centT_in, ebias_in, wrT_in, br_in,
          wsT_in, bs_in, const_in, out):
    f32, bf16, i32, u32 = mybir.dt.float32, mybir.dt.bfloat16, mybir.dt.int32, mybir.dt.uint32
    ALU, ACT, AX = mybir.AluOpType, mybir.ActivationFunctionType, mybir.AxisListType
    ds = bass.ds

    lists = nc.dram_tensor("lists", [DUMMY + P, ROW], f32, kind="Internal").ap()
    y_dram = nc.dram_tensor("y", [YROWS, D], f32, kind="Internal").ap()

    with ExitStack() as ctx:
        def sb(name, shape, dt=f32):
            return ctx.enter_context(nc.sbuf_tensor(name, shape, dt))

        def pb(name, shape):
            return ctx.enter_context(nc.psum_tensor(name, shape, f32))

        def sem(name):
            return ctx.enter_context(nc.semaphore(name))

        const = sb("const", [P, NCONST])
        x = sb("x", [P, TILES, D])
        wq, wk, wv, wo = (sb(n, [P, DC, D]) for n in ("wq", "wk", "wv", "wo"))
        ws = sb("ws", [P, SHARED, DC, D])
        wsr = sb("wsr", [P, DC, D + EXPERTS])
        bsr = sb("bsr", [1, SHARED, D])
        brow = sb("brow", [1, D + EXPERTS])
        wr = sb("wr", [P, DC, EXPERTS * D])
        br = sb("br", [P, EXPERTS * D])
        ctxT = sb("ctxT", [P, DC, BATCH, NKEYS])
        ctxrep = sb("ctxrep", [P, DC, BATCH, CH * P])
        lens = sb("lens", [P, BATCH], i32)
        lensf = sb("lensf", [P, BATCH])
        empty = sb("empty", [P, BATCH])
        lenkeep = sb("lenkeep", [P, BATCH])
        valid = sb("valid", [P, BATCH, NKEYS])
        filler = sb("filler", [P, BATCH, NKEYS])
        keep = sb("keep", [P, BATCH, CH])
        kT = sb("kT", [P, BATCH, NKEYS])
        kTm = sb("kTm", [P, BATCH, NKEYS])
        kTf = sb("kTf", [P, BATCH, NKEYS])
        kblock = sb("kblock", [P, BATCH, DC, HALF])
        vblock = sb("vblock", [P, BATCH, CH, SPAN, ODIM])
        ones = sb("ones", [P, P])
        before16 = sb("before16", [P, P], bf16)
        ones16 = sb("ones16", [P, P], bf16)
        stats = sb("stats", [P, TILES, 6])
        mv = sb("mv", [P, TILES, 2])
        power = sb("power", [P, 4])
        eps = sb("eps", [P, 1])
        carried = sb("carried", [P, 2])
        veps = sb("veps", [P, TILES])
        rstd = sb("rstd", [P, TILES])
        veps2 = sb("veps2", [P, 1])
        xn = sb("xn", [P, 2, D])
        xnT = sb("xnT", [P, DC, 2, P])
        qT = sb("qT", [P, DC, 2, P])
        rowmax = sb("rowmax", [P, 2, HEADS])
        s_sb = [sb(f"s_sb{i}", [P, CH * P]) for i in range(2)]
        pT = [sb(f"pT{i}", [P, CH, P]) for i in range(2)]
        rden = sb("rden", [P, HEADS])
        o_sb = [sb(f"o_sb{i}", [P, D]) for i in range(2)]
        oT = sb("oT", [P, DC, P])
        stats2 = sb("stats2", [P, 6])
        mv2 = [sb(f"mv2_{i}", [P, 2]) for i in range(2)]
        rstd2 = [sb(f"rstd2_{i}", [P, 1]) for i in range(2)]
        urow = [[sb(f"urow{i}{c}", [P, ROW]) for c in range(TOPK)] for i in range(2)]
        uT = [sb(f"uT{i}", [P, DC, P]) for i in range(2)]
        ids = sb("ids", [P, TILES, TOPK], i32)
        logits = sb("logits", [P, TILES, EXPERTS])
        top2 = sb("top2", [P, TILES, TOPK])
        logit = [sb(f"logit{i}", [P, EXPERTS]) for i in range(2)]
        top8 = [sb(f"top8_{i}", [P, 8]) for i in range(2)]
        idx8 = sb("idx8", [P, 8], u32)
        idxf = sb("idxf", [P, TOPK])
        onehot = sb("onehot", [P, TOPK, EXPERTS])
        chosen = sb("chosen", [P, EXPERTS], bf16)
        seen = sb("seen", [P, EXPERTS], bf16)
        place = sb("place", [P, EXPERTS])
        placed = sb("placed", [P, TOPK, EXPERTS])
        posf = sb("posf", [P, TOPK])
        pos = [sb(f"pos{i}", [P, TOPK], i32) for i in range(2)]
        shifted = sb("shifted", [P, TILES, EXPERTS])
        second = sb("second", [P, TILES])
        gsum = sb("gsum", [P, TILES])
        gate = sb("gate", [P, TOPK, TILES])
        count = sb("count", [1, EXPERTS])
        over = sb("over", [1, EXPERTS, EXPERTS])
        ntiles = sb("ntiles", [1, EXPERTS])
        upto = sb("upto", [1, EXPERTS, EXPERTS])
        lasttile = sb("lasttile", [1, EXPERTS])
        skip = sb("skip", [1, EXPERTS])
        passed = sb("passed", [1, LISTS, EXPERTS])
        skipped = sb("skipped", [1, LISTS, EXPERTS])
        expert = sb("expert", [1, LISTS])
        start = sb("start", [1, LISTS])
        fill = sb("fill", [1, EXPERTS])
        expert_i = sb("expert_i", [1, LISTS], i32)
        start_i = sb("start_i", [1, LISTS], i32)
        fill_i = sb("fill_i", [1, EXPERTS], i32)
        padblock = sb("padblock", [P, ROW])
        NB = 4
        lrow = [sb(f"lrow{j}", [P, ROW]) for j in range(NB)]
        yrow = [sb(f"yrow{j}", [P, D]) for j in range(NB)]
        ysum = wr[:, :, :].rearrange("p c n -> p (c n)").rearrange("p (t c d) -> p t c d", t=TILES, c=TOPK)
        part = sb("part", [P, 2, D])

        S = [pb(f"S{h}", [P, 2, 512]) for h in range(2)]
        T = pb("T", [P, 4, P])
        A = pb("A", [P, 4, P])
        B = pb("B", [P, 512])
        O = pb("O", [P, 512])
        A2 = A[:, 0:DC, :]

        def cst(name, parts=P):
            return const[0:parts, slice(*_COLS[name])]

        ident = cst("ident")

        names = ("const", "len", "ctx", "wk", "wv", "wq", "wo", "ws", "bsr", "cent", "ebias", "wr", "br")
        arrived = {n: sem("arrived_" + n) for n in names}
        x_arrived = [sem(f"x_arrived{g}") for g in range(4)]
        pool_set, dve_chain = sem("pool_set"), sem("dve_chain")
        veps_ready, rstd_ready, veps2_ready, rstd2_ready = sem("veps_ready"), sem("rstd_ready"), sem("veps2_ready"), sem("rstd2_ready")
        pool_carried = sem("pool_carried")
        u_copied, id_ready, kept = sem("u_copied"), sem("id_ready"), sem("kept")
        rep_ready = sem("rep_ready")
        kproj, kproj_taken, kblock_ready = sem("kproj"), sem("kproj_taken"), sem("kblock_ready")
        vproj, vblock_ready, wsr_ready = sem("vproj"), sem("vblock_ready"), sem("wsr_ready")
        ln1_ready, xn_ready, xT_psum, xT_ready = sem("ln1_ready"), sem("xn_ready"), sem("xT_psum"), sem("xT_ready")
        q_psum, q_ready = sem("q_psum"), sem("q_ready")
        s_psum, s_ready = sem("s_psum"), sem("s_ready")
        t_psum, p_ready = sem("t_psum"), sem("p_ready")
        o_psum, o_ready = sem("o_psum"), sem("o_ready")
        oT_psum, oT_ready = sem("oT_psum"), sem("oT_ready")
        out_psum, out_taken, ln2_ready = sem("out_psum"), sem("out_taken"), sem("ln2_ready")
        u_ready, uT_psum, uT_ready = sem("u_ready"), sem("uT_psum"), sem("uT_ready")
        r_psum, r_taken, chosen_ready = sem("r_psum"), sem("r_taken"), sem("chosen_ready")
        rank_psum, pos_ready = sem("rank_psum"), sem("pos_ready")
        scattered = [sem(f"scattered{i}") for i in range(4)]
        count_psum, table_ready, gate_ready, exps_ready = sem("count_psum"), sem("table_ready"), sem("gate_ready"), sem("exps_ready")
        shifted_ready = sem("shifted_ready")
        filled = [sem(f"filled{i}") for i in range(EXPERTS)]
        dummy_written = sem("dummy_written")
        l_arrived = [sem(f"l_arrived{j}") for j in range(NB)]
        y_back = [sem(f"y_back{g}") for g in range(4)]
        out_ready = sem("out_ready")
        stored = [sem(f"stored{g}") for g in range(4)]

        FIRST, LAST = 4, 14

        def slots(eng, slot):
            for s in range(-1, FIRST):
                slot(s, s % 2)
            with eng.Fori(FIRST, LAST, 2) as s:
                slot(s, 0)
                slot(s + 1, 1)
            for s in range(LAST, TILES + 2):
                slot(s, s % 2)

        def has(s, tile):
            return not isinstance(s, int) or 0 <= tile < TILES

        def after(s, n):
            return not isinstance(s, int) or s >= n

        def opening(s):
            return isinstance(s, int) and s == -1

        def half_of(n):
            return n // 2

        def carry(eng, column):
            return eng.tensor_tensor(carried[:, column:column + 1], power[:, 0:1], power[:, 0:1], ALU.add)

        block = ctx.enter_context(nc.Block())

        @block.sync
        def _(sp):
            def load(to, of, name):
                sp.dma_start(to, of).then_inc(arrived[name], 16)

            load(const[:, :], const_in, "const")
            load(lens[:, :], lens_in.rearrange("(o b) -> o b", o=1).to_broadcast([P, BATCH]), "len")
            load(ctxT[:, :, :, :], ctxT_in.rearrange("(c p) b k -> p c b k", p=P), "ctx")
            load(wk[:, :, :], wk_in.rearrange("(c p) n -> p c n", p=P), "wk")
            load(wq[:, :, :], wq_in.rearrange("(c p) n -> p c n", p=P), "wq")
            load(wv[:, :, :], wv_in.rearrange("(c p) n -> p c n", p=P), "wv")
            load(wo[:, :, :], wo_in.rearrange("(c p) n -> p c n", p=P), "wo")
            for n in range(SHARED):
                sp.dma_start(ws[:, n, :, :], wsT_in[:, n, :].rearrange("(c p) n -> p c n", p=P)).then_inc(arrived["ws"], 16)
            load(bsr[:, :, :], bs_in.rearrange("(o s) n -> o s n", o=1), "bsr")
            load(wr[:, :, :], wrT_in.rearrange("(c p) n -> p c n", p=P), "wr")
            load(br[:, :], br_in.rearrange("(o e) n -> o (e n)", o=1).to_broadcast([P, EXPERTS * D]), "br")
            sp.wait_ge(pool_set, 1)
            sp.dma_start(lists[DUMMY:DUMMY + P, :], padblock[:, :]).then_inc(dummy_written, 16)
            sp.wait_ge(table_ready, 1)
            for n in range(0, EXPERTS, 2):
                row = sp.value_load(fill_i[0:1, n:n + 1], min_val=0, max_val=DUMMY - P)
                sp.dma_start(lists[ds(row, P), :], padblock[:, :]).then_inc(filled[n], 16)
            for n in range(EXPERTS):
                sp.wait_ge(filled[n], 16)
            sp.wait_ge(dummy_written, 16)
            for j in range(4):
                sp.wait_ge(scattered[j], TILES // 2 * 16)
            with sp.Fori(0, LISTS // NB) as i:
                for j in range(NB):
                    row = sp.value_load(start_i[0:1, ds(i * NB + j, 1)], min_val=0, max_val=DUMMY)
                    sp.wait_ge(scattered[j], TILES // 2 * 16 + i * 16)
                    sp.dma_start(lrow[j][:, :], lists[ds(row, P), :]).then_inc(l_arrived[j], 16)
            for j in range(NB):
                sp.wait_ge(scattered[j], (TILES // 2 + LISTS // NB) * 16)
            for g in range(4):
                for c in range(TOPK):
                    sp.dma_start(ysum[:, 4 * g:4 * g + 4, c, :],
                                 y_dram[c * TOKENS + g * 4 * P:c * TOKENS + (g + 1) * 4 * P, :]
                                 .rearrange("(t p) d -> p t d", p=P)).then_inc(y_back[g], 16)
            for g in range(4):
                sp.wait_ge(stored[g], 16)

        @block.scalar
        def _(act):
            for g in range(4):
                act.dma_start(x[:, 4 * g:4 * g + 4, :],
                              x_in[g * 4 * P:(g + 1) * 4 * P, :].rearrange("(t p) d -> p t d", p=P)
                              ).then_inc(x_arrived[g], 16)
            act.dma_start(wsr[:, :, D:D + EXPERTS],
                          centT_in.rearrange("(c p) e -> p c e", p=P)).then_inc(arrived["cent"], 16)
            act.dma_start(brow[:, D:D + EXPERTS],
                          ebias_in.rearrange("(o e) -> o e", o=1)).then_inc(arrived["ebias"], 16)

            act.wait_ge(arrived["ctx"], 16)
            for c in range(DC):
                for b in range(BATCH):
                    nc.scalar.activation(ctxrep[:, c, b, 0:ROWS].rearrange("p (h k) -> p h k", k=NKEYS),
                                         ctxT[:, c, b, :].unsqueeze(1).to_broadcast([P, HEADS, NKEYS]),
                                         ACT.Copy).then_inc(rep_ready, 1)

            def exps(s, par, g):
                c0, c1 = GROUPS[g]
                act.wait_ge(t_psum, 3 * s + g + 1)
                if g == 0 and (after(s, 2)):
                    act.wait_ge(o_psum, s - 1)
                nc.scalar.activation(pT[par][:, c0:c1, :], T[:, 0:c1 - c0, :], ACT.Exp).then_inc(p_ready, 1)

            def project_queries(s, pair):
                act.wait_ge(xT_psum, pair + 1)
                if not isinstance(pair, int) or pair >= 1:
                    act.wait_ge(q_psum, pair)
                nc.scalar.activation(xnT[:, :, :, :].rearrange("p c t n -> p (c t) n"), A[:, :, :],
                                     ACT.Copy).then_inc(xT_ready, 1)

            def take_queries(s, pair):
                act.wait_ge(q_psum, pair + 1)
                if has(s, s):
                    act.wait_ge(s_psum, 2 * s + 4)
                nc.scalar.activation(qT[:, :, :, :].rearrange("p c t n -> p (c t n)"), B[:, :],
                                     ACT.Copy).then_inc(q_ready, 1)

            def slot(s, par):
                if has(s, s):
                    exps(s, par, 0)
                if has(s, s - 1):
                    act.wait_ge(oT_psum, s)
                    if after(s, 2):
                        act.wait_ge(out_psum, s - 1)
                    nc.scalar.activation(oT[:, :, :], A2, ACT.Copy).then_inc(oT_ready, 1)
                if has(s, s):
                    exps(s, par, 1)
                    exps(s, par, 2)
                if opening(s):
                    project_queries(s, 0)
                    take_queries(s, 0)
                elif par == 0 and has(s, s + 2):
                    project_queries(s, half_of(s) + 1)
                if has(s, s - 1):
                    act.wait_ge(u_ready, s)
                    if after(s, 3):
                        act.wait_ge(scattered[2 * (1 - par) + 1], 16 * half_of(s - 1))
                    nc.scalar.activation(urow[1 - par][1][:, 0:D], urow[1 - par][0][:, 0:D], ACT.Copy).then_inc(u_copied, 1)
                    act.wait_ge(uT_psum, s)
                    if after(s, 3):
                        act.wait_ge(r_psum, s - 2)
                    nc.scalar.activation(uT[1 - par][:, :, :], A2, ACT.Copy).then_inc(uT_ready, 1)
                if not opening(s) and par == 0 and has(s, s + 2):
                    take_queries(s, half_of(s) + 1)

            slots(act, slot)
            act.wait_ge(table_ready, 1)
            for n in range(1, EXPERTS, 2):
                row = act.value_load(fill_i[0:1, n:n + 1], min_val=0, max_val=DUMMY - P)
                act.dma_start(lists[ds(row, P), :], padblock[:, :]).then_inc(filled[n], 16)
            act.wait_ge(shifted_ready, 2)
            nc.scalar.activation(shifted[:, :, :], shifted[:, :, :], ACT.Exp).then_inc(exps_ready, 1)
            nc.scalar.activation(second[:, :], second[:, :], ACT.Exp).then_inc(exps_ready, 1)
            with act.Fori(0, LISTS // NB) as i:
                for j in range(NB):
                    k = i * NB + j
                    act.wait_ge(uT_psum, TILES + k + 1)
                    act.wait_ge(out_psum, TILES + k - 1)
                    nc.scalar.activation(uT[j % 2][:, :, :], S[j % 2][:, 0, 0:D].rearrange("p (c n) -> p c n", c=DC),
                                         ACT.Copy).then_inc(uT_ready, 1)
            for g in range(4):
                act.wait_ge(out_ready, 4 * (g + 1))
                act.dma_start(out[g * 4 * P:(g + 1) * 4 * P, :].rearrange("(t p) d -> p t d", p=P),
                              x[:, 4 * g:4 * g + 4, :]).then_inc(stored[g], 16)

        @block.gpsimd
        def _(pool):
            nc.gpsimd.memset(padblock[:, 0:D], 0.0)
            nc.gpsimd.memset(padblock[:, D:ROW].bitcast(i32), PADROW).then_inc(pool_set, 1)
            nc.gpsimd.memset(ones[:, :], 1.0)
            nc.gpsimd.memset(power[:, :], -0.5)
            nc.gpsimd.memset(eps[:, :], EPS)
            nc.gpsimd.memset(ones16[:, :], 1.0)
            nc.gpsimd.memset(seen[:, :], 0.0)
            for i in range(2):
                nc.gpsimd.memset(s_sb[i][:, ROWS:CH * P], 0.0)
            nc.gpsimd.memset(ctxrep[:, :, :, ROWS:CH * P], 0.0).then_inc(pool_set, 1)
            pool.wait_ge(arrived["const"], 16)
            nc.gpsimd.tensor_copy(before16[:, :], cst("before"))
            nc.gpsimd.tensor_copy(ids[:, :, :].rearrange("p t c -> p (t c)"), cst("ids")).then_inc(pool_set, 1)
            pool.wait_ge(pool_set, 3)

            for g in range(4):
                four = slice(4 * g, 4 * g + 4)
                pool.wait_ge(ln1_ready, g + 1)
                nc.gpsimd.tensor_scalar(veps[:, four], mv[:, four, 1], EPS, None, ALU.add).then_inc(veps_ready, 1)
                pool.wait_ge(veps_ready, g + 1)
                nc.gpsimd.tensor_tensor(rstd[:, four], veps[:, four], power[:, :], ALU.pow).then_inc(rstd_ready, 1)

            def slot(s, par):
                if has(s, s - 2):
                    pool.wait_ge(chosen_ready, s - 1)
                    nc.gpsimd.tensor_copy(logits[:, ds(s - 2, 1), :].rearrange("p a e -> p (a e)"), logit[par][:, :])
                    nc.gpsimd.tensor_copy(top2[:, ds(s - 2, 1), :].rearrange("p a e -> p (a e)"),
                                          top8[par][:, 0:TOPK]).then_inc(kept, 1)
                if has(s, s - 1):
                    t, q = s - 1, 1 - par
                    pool.wait_ge(ln2_ready, s)
                    nc.gpsimd.tensor_tensor(veps2[:, :], mv2[q][:, 1:2], eps[:, :], ALU.add).then_inc(veps2_ready, 1)
                    pool.wait_ge(veps2_ready, s)
                    nc.gpsimd.tensor_tensor(rstd2[q][:, :], veps2[:, :], power[:, 0:1], ALU.pow).then_inc(rstd2_ready, 1)
                    if after(s, 3):
                        for c in range(TOPK):
                            pool.wait_ge(scattered[2 * q + c], 16 * half_of(s - 1))
                    for c in range(TOPK):
                        last = nc.gpsimd.tensor_copy(urow[q][c][:, D:ROW].bitcast(i32), ids[:, ds(t, 1), c])
                    last.then_inc(id_ready, 1)
                if has(s, s - 2):
                    pool.wait_ge(pos_ready, s - 1)
                    pool.wait_ge(id_ready, s - 1)
                    pool.wait_ge(u_copied, s - 1)
                    if after(s, 3):
                        pool.wait_ge(pool_carried, s - 2)
                    carry(pool, 1).then_inc(pool_carried, 1)
                    for c in range(TOPK):
                        nc.gpsimd.indirect_dma_start(
                            out=lists, out_offset=bass.IndirectOffsetOnAxis(ap=pos[par][:, c:c + 1], axis=0),
                            in_=urow[par][c][:, :], in_offset=None).then_inc(scattered[2 * par + c], 16)

            slots(pool, slot)
            with pool.Fori(0, LISTS // NB) as i:
                for j in range(NB):
                    k = i * NB + j
                    pool.wait_ge(out_taken, TILES + k + 1)
                    pool.wait_ge(l_arrived[j], 16 * i + 16)
                    pool.wait_ge(pool_carried, TILES + k)
                    carry(pool, 1).then_inc(pool_carried, 1)
                    nc.gpsimd.indirect_dma_start(
                        out=y_dram, out_offset=bass.IndirectOffsetOnAxis(ap=lrow[j][:, D:ROW].bitcast(i32), axis=0),
                        in_=yrow[j][:, :], in_offset=None, bounds_check=YROWS - 1, oob_is_err=False
                        ).then_inc(scattered[j], 16)

        @block.vector
        def _(dve):
            class Chain:
                base, n = 0, 0

            def link(ins):
                Chain.n += 1
                ins.then_inc(dve_chain, 1)
                dve.wait_ge(dve_chain, Chain.base + Chain.n)

            def flat(ap):
                return ap.rearrange("p a d -> p (a d)")

            V = nc.vector
            dve.wait_ge(arrived["const"], 16)
            dve.wait_ge(arrived["len"], 16)
            link(V.tensor_copy(lensf[:, :], lens[:, :]))
            link(V.tensor_scalar(empty[:, :], lensf[:, :], 0.0, None, ALU.is_le))
            link(V.scalar_tensor_tensor(out=lenkeep[:, :], in0=empty[:, :], scalar=float(NKEYS), in1=lensf[:, :],
                                        op0=ALU.mult, op1=ALU.max))
            for b in range(BATCH):
                V.tensor_scalar(keep[:, b, :], cst("rowkey"), lenkeep[:, b:b + 1], None, ALU.is_lt)
                link(V.tensor_scalar(valid[:, b, :], cst("key"), lensf[:, b:b + 1], None, ALU.is_lt))
                link(V.tensor_scalar(filler[:, b, :], valid[:, b, :], -1.0, 1.0, ALU.mult, ALU.add))
                link(V.tensor_scalar(filler[:, b, :], filler[:, b, :], empty[:, b:b + 1], None, ALU.subtract))

            def ln1(g):
                dve.wait_ge(x_arrived[g], 16)
                for t in range(4 * g, 4 * g + 4):
                    last = V.bn_stats(stats[:, t, :], x[:, t, :])
                link(last)
                for t in range(4 * g, 4 * g + 4):
                    last = V.bn_aggr(mv[:, t, :], stats[:, t, :])
                last.then_inc(ln1_ready, 1)

            ln1(0)
            for c in range(DC):
                dve.wait_ge(kproj, DC)
                link(V.tensor_copy(kT[:, :, :], B[:, 256 * c:256 * c + BATCH * NKEYS].rearrange("p (b k) -> p b k", b=BATCH)))
                V.tensor_tensor(kTf[:, :, :], filler[:, :, :], kT[:, :, 0:1].to_broadcast([P, BATCH, NKEYS]), ALU.mult)
                link(V.tensor_tensor(kTm[:, :, :], valid[:, :, :], kT[:, :, :], ALU.mult))
                link(V.tensor_tensor(kTm[:, :, :], kTm[:, :, :], kTf[:, :, :], ALU.add))
                for b in range(BATCH):
                    last = V.tensor_tensor(
                        kblock[:, b, c, :].rearrange("p (h k) -> p h k", k=NKEYS),
                        kTm[:, b, :].unsqueeze(1).to_broadcast([P, HEADS // 2, NKEYS]),
                        cst("headmask").unsqueeze(2).to_broadcast([P, HEADS // 2, NKEYS]), ALU.mult)
                last.then_inc(kblock_ready, 1)
            for b in range(BATCH):
                last = V.tensor_tensor(vblock[:, b, :, :, DH], cst("rowhead").rearrange("p (c s) -> p c s", s=SPAN),
                                       keep[:, b, :].unsqueeze(2).to_broadcast([P, CH, SPAN]), ALU.mult)
            link(last)
            for b in range(BATCH):
                dve.wait_ge(vproj, b + 1)
                bank = (T[:, :, :].rearrange("p a n -> p (a n)"), O[:, :])[b]
                last = V.tensor_tensor(
                    vblock[:, b, :, :, 0:DH],
                    bank[:, 0:CH * SPAN * DH].rearrange("p (c s j) -> p c s j", s=SPAN, j=DH),
                    vblock[:, b, :, :, DH:ODIM].to_broadcast([P, CH, SPAN, DH]), ALU.mult)
                last.then_inc(vblock_ready, 1)
            dve.wait_ge(arrived["ws"], 16 * SHARED)
            dve.wait_ge(arrived["bsr"], 16)
            V.tensor_tensor(wsr[:, :, 0:D], ws[:, 0, :, :], ws[:, 1, :, :], ALU.add)
            link(V.tensor_tensor(brow[:, 0:D], bsr[:, 0, :], bsr[:, 1, :], ALU.add))
            V.tensor_scalar(wsr[:, :, 0:D], wsr[:, :, 0:D], 1.0 / SHARED, None, ALU.mult)
            link(V.tensor_scalar(brow[:, 0:D], brow[:, 0:D], 1.0 / SHARED, None, ALU.mult))
            for c in range(DC):
                last = V.tensor_tensor(wsr[:, c, c * P:(c + 1) * P], wsr[:, c, c * P:(c + 1) * P], ident, ALU.add)
            last.then_inc(wsr_ready, 1)
            for g in range(1, 4):
                ln1(g)

            def score(s, half, par):
                t = s + 1
                dve.wait_ge(s_psum, 2 * t + half + 1)
                if after(s, 1):
                    dve.wait_ge(t_psum, 3 * s - 3 + 3)
                sc = S[half][:, :, 0:QUART].rearrange("p b (h k) -> p b h k", k=NKEYS)
                mx = rowmax[:, half, 0:8]
                link(V.tensor_reduce(mx.rearrange("p (b h) -> p b h", b=2), sc, AX.X, ALU.max))
                V.tensor_tensor(
                    s_sb[par][:, half * HALF:(half + 1) * HALF].rearrange("p (b h k) -> p b h k", b=2, k=NKEYS), sc,
                    mx.rearrange("p (b h) -> p b h", b=2).unsqueeze(3).to_broadcast([P, 2, 4, NKEYS]),
                    ALU.subtract).then_inc(s_ready, 1)

            def normalise(s, pair):
                dve.wait_ge(rstd_ready, pair // 2 + 1 if isinstance(pair, int) else 4)
                if not isinstance(pair, int) or pair >= 1:
                    dve.wait_ge(xT_psum, pair)
                for n in range(2):
                    t = 2 * pair + n
                    last = V.tensor_scalar(xn[:, n, :], flat(x[:, ds(t, 1), :]), mv[:, ds(t, 1), 0], rstd[:, ds(t, 1)],
                                           ALU.subtract, ALU.mult)
                last.then_inc(xn_ready, 1)

            def slot(s, par):
                if opening(s):
                    normalise(s, 0)
                elif par == 0 and has(s, s + 2):
                    normalise(s, half_of(s) + 1)
                if has(s, s - 2):
                    t = s - 2
                    dve.wait_ge(r_psum, s - 1)
                    if after(s, 4):
                        dve.wait_ge(kept, s - 3)
                    link(V.tensor_copy(logit[par][:, :], B[:, D:D + EXPERTS]))
                    V.tensor_tensor(flat(x[:, ds(t, 1), :]), B[:, 0:D], flat(x[:, ds(t, 1), :]), ALU.add).then_inc(r_taken, 1)
                    link(V.max(top8[par][:, :], logit[par][:, :]))
                    carry(dve, 0)
                    link(V.max_index(idx8[:, :], top8[par][:, :], logit[par][:, :]))
                    link(V.tensor_copy(idxf[:, :], idx8[:, 0:TOPK]))
                    link(V.tensor_tensor(onehot[:, :, :], cst("expert").unsqueeze(1).to_broadcast([P, TOPK, EXPERTS]),
                                         idxf[:, :].unsqueeze(2).to_broadcast([P, TOPK, EXPERTS]), ALU.is_equal))
                    V.tensor_tensor(chosen[:, :], onehot[:, 0, :], onehot[:, 1, :], ALU.add).then_inc(chosen_ready, 1)
                if has(s, s + 1):
                    score(s, 0, 1 - par)
                if has(s, s - 1):
                    t, q = s - 1, 1 - par
                    dve.wait_ge(out_psum, s)
                    V.tensor_tensor(flat(x[:, ds(t, 1), :]), B[:, 0:D], flat(x[:, ds(t, 1), :]),
                                    ALU.add).then_inc(out_taken, 1)
                    dve.wait_ge(out_taken, s)
                    carry(dve, 0)
                    link(V.bn_stats(stats2[:, :], flat(x[:, ds(t, 1), :])))
                    carry(dve, 0)
                    V.bn_aggr(mv2[q][:, :], stats2[:, :]).then_inc(ln2_ready, 1)
                if has(s, s + 1):
                    score(s, 1, 1 - par)
                if has(s, s - 1):
                    dve.wait_ge(rstd2_ready, s)
                    if after(s, 3):
                        dve.wait_ge(scattered[2 * q], 16 * half_of(s - 1))
                        dve.wait_ge(u_copied, s - 2)
                        dve.wait_ge(uT_psum, s - 2)
                    V.tensor_scalar(urow[q][0][:, 0:D], flat(x[:, ds(t, 1), :]), mv2[q][:, 0:1], rstd2[q][:, 0:1],
                                    ALU.subtract, ALU.mult).then_inc(u_ready, 1)
                if has(s, s - 2):
                    dve.wait_ge(rank_psum, s - 1)
                    link(V.tensor_tensor(place[:, :], B[:, 0:EXPERTS], cst("region"), ALU.add))
                    V.tensor_tensor(seen[:, :], seen[:, :], chosen[:, :], ALU.add)
                    link(V.tensor_tensor(placed[:, :, :], onehot[:, :, :],
                                         place[:, :].unsqueeze(1).to_broadcast([P, TOPK, EXPERTS]), ALU.mult))
                    link(V.tensor_reduce(posf[:, :], placed[:, :, :], AX.X, ALU.add))
                    if after(s, 4):
                        for c in range(TOPK):
                            dve.wait_ge(scattered[2 * par + c], 16 * half_of(s - 2))
                    V.tensor_copy(pos[par][:, :], posf[:, :]).then_inc(pos_ready, 1)
                if has(s, s):
                    dve.wait_ge(o_psum, s + 1)
                    if after(s, 2):
                        dve.wait_ge(oT_psum, s - 1)
                    oh = O[:, 0:HEADS * ODIM].rearrange("p (h j) -> p h j", j=ODIM)
                    link(V.reciprocal(rden[:, :], oh[:, :, DH]))
                    V.tensor_tensor(o_sb[par][:, :].rearrange("p (h j) -> p h j", j=DH), oh[:, :, 0:DH],
                                    rden[:, :].unsqueeze(2).to_broadcast([P, HEADS, DH]), ALU.mult).then_inc(o_ready, 1)

            for s in range(-1, FIRST - 2):
                slot(s, s % 2)
            per_two = -Chain.n
            for s in range(FIRST - 2, FIRST):
                slot(s, s % 2)
            before_loop = Chain.n
            per_two += Chain.n
            with dve.Fori(FIRST, LAST, 2) as s:
                Chain.base, Chain.n = (s - FIRST) * (per_two // 2) + before_loop, 0
                slot(s, 0)
                slot(s + 1, 1)
                assert Chain.n == per_two, Chain.n
            Chain.base, Chain.n = 0, before_loop + per_two * (LAST - FIRST) // 2
            for s in range(LAST, TILES + 2):
                slot(s, s % 2)

            dve.wait_ge(count_psum, 1)
            e1 = [1, EXPERTS, EXPERTS]
            link(V.tensor_copy(count[:, :], B[0:1, 0:EXPERTS]))
            V.tensor_tensor(fill[:, :], count[:, :], cst("region", 1), ALU.add)
            link(V.tensor_tensor(over[:, :, :], count[:, :].unsqueeze(2).to_broadcast(e1),
                                 cst("tilerows", 1).unsqueeze(1).to_broadcast(e1), ALU.is_gt))
            V.tensor_copy(fill_i[:, :], fill[:, :])
            link(V.tensor_reduce(ntiles[:, :], over[:, :, :], AX.X, ALU.add))
            V.tensor_scalar(skip[:, :], ntiles[:, :], -float(P), float(REGION), ALU.mult, ALU.add)
            link(V.tensor_tensor(upto[:, :, :], ntiles[:, :].unsqueeze(1).to_broadcast(e1),
                                 cst("upto", 1).rearrange("p (a b) -> p a b", b=EXPERTS), ALU.mult))
            link(V.tensor_reduce(lasttile[:, :], upto[:, :, :], AX.X, ALU.add))
            k1 = [1, LISTS, EXPERTS]
            link(V.tensor_tensor(passed[:, :, :], lasttile[:, :].unsqueeze(1).to_broadcast(k1),
                                 cst("lists", 1).unsqueeze(2).to_broadcast(k1), ALU.is_le))
            V.tensor_reduce(expert[:, :], passed[:, :, :], AX.X, ALU.add)
            link(V.tensor_tensor(skipped[:, :, :], passed[:, :, :], skip[:, :].unsqueeze(1).to_broadcast(k1), ALU.mult))
            V.tensor_scalar(expert[:, :], expert[:, :], float(EXPERTS - 1), float(D), ALU.min, ALU.mult)
            link(V.tensor_reduce(start[:, :], skipped[:, :, :], AX.X, ALU.add))
            V.tensor_copy(expert_i[:, :], expert[:, :])
            link(V.scalar_tensor_tensor(out=start[:, :], in0=cst("lists", 1), scalar=float(P), in1=start[:, :],
                                        op0=ALU.mult, op1=ALU.add))
            link(V.tensor_scalar(start[:, :], start[:, :], float(DUMMY), None, ALU.min))
            V.tensor_copy(start_i[:, :], start[:, :]).then_inc(table_ready, 1)

            dve.wait_ge(kept, TILES)
            V.tensor_tensor(shifted[:, :, :], logits[:, :, :], top2[:, :, 0:1].to_broadcast([P, TILES, EXPERTS]),
                            ALU.subtract).then_inc(shifted_ready, 1)
            V.tensor_tensor(second[:, :], top2[:, :, 1], top2[:, :, 0], ALU.subtract).then_inc(shifted_ready, 1)
            dve.wait_ge(exps_ready, 2)
            link(V.tensor_reduce(gsum[:, :], shifted[:, :, :], AX.X, ALU.add))
            link(V.reciprocal(gate[:, 0, :], gsum[:, :]))
            link(V.tensor_tensor(gate[:, 1, :], second[:, :], gate[:, 0, :], ALU.mult))

            dve.wait_ge(table_ready, 1)
            dve.wait_ge(arrived["br"], 16)
            with dve.Fori(0, LISTS // NB) as i:
                cols = [dve.value_load(expert_i[0:1, ds(i * NB + j, 1)], min_val=0, max_val=(EXPERTS - 1) * D)
                        for j in range(NB)]
                for j in range(NB):
                    k = i * NB + j
                    dve.wait_ge(out_psum, TILES + k + 1)
                    dve.wait_ge(scattered[j], TILES // 2 * 16 + i * 16)
                    V.tensor_tensor(yrow[j][:, :], S[j % 2][:, 1, 0:D], br[:, ds(cols[j], D)], ALU.add).then_inc(out_taken, 1)

            combine_base = Chain.n
            for g in range(4):
                dve.wait_ge(y_back[g], 16 * TOPK)
                with dve.Fori(0, 4) as i:
                    t = i + 4 * g
                    V.scalar_tensor_tensor(out=part[:, 0, :], in0=flat(ysum[:, ds(t, 1), 0, :]), scalar=gate[:, 0, ds(t, 1)],
                                           in1=flat(x[:, ds(t, 1), :]), op0=ALU.mult, op1=ALU.add).then_inc(dve_chain, 1)
                    dve.wait_ge(dve_chain, t + combine_base + 1)
                    V.scalar_tensor_tensor(out=flat(x[:, ds(t, 1), :]), in0=flat(ysum[:, ds(t, 1), 1, :]),
                                           scalar=gate[:, 1, ds(t, 1)], in1=part[:, 0, :],
                                           op0=ALU.mult, op1=ALU.add).then_inc(out_ready, 1)
                    dve.wait_ge(out_ready, t + 1)

        @block.tensor
        def _(pe):
            M = nc.tensor.matmul

            def transpose(o, i):
                return M(o, i, ident, start=True, stop=True, is_transpose=True)

            pe.wait_ge(arrived["const"], 16)
            pe.wait_ge(arrived["ctx"], 16)
            pe.wait_ge(arrived["wk"], 16)
            for h in range(DC):
                for c in range(DC):
                    last = M(B[:, 256 * h:256 * h + BATCH * NKEYS], wk[:, c, h * P:(h + 1) * P],
                             ctxT[:, c, :, :].rearrange("p b k -> p (b k)"), start=(c == 0), stop=(c == DC - 1))
                last.then_inc(kproj, 1)
            pe.wait_ge(arrived["wv"], 16)
            pe.wait_ge(rep_ready, DC * BATCH)
            pe.wait_ge(pool_set, 3)
            for b in range(BATCH):
                bank = (T[:, :, :].rearrange("p a n -> p (a n)"), O[:, :])[b]
                w = SPAN * DH
                for ch in range(CH):
                    for c in range(DC):
                        last = M(bank[:, ch * w:(ch + 1) * w], ctxrep[:, c, b, ch * P:(ch + 1) * P],
                                 wv[:, c, HEAD0[ch] * DH:HEAD0[ch] * DH + w], start=(c == 0), stop=(c == DC - 1))
                last.then_inc(vproj, 1)

            def transpose_x(s, pair):
                pe.wait_ge(xn_ready, pair + 1)
                if has(s, s - 1):
                    pe.wait_ge(oT_ready, s)
                for n in range(2):
                    for c in range(DC):
                        last = transpose(A[:, 2 * c + n, :], xn[:, n, c * P:(c + 1) * P])
                last.then_inc(xT_psum, 1)

            def queries(s, pair):
                pe.wait_ge(xT_ready, pair + 1)
                if opening(s):
                    pe.wait_ge(kblock_ready, DC)
                if has(s, s - 2):
                    pe.wait_ge(pos_ready, s - 1)
                elif has(s, s - 1):
                    pe.wait_ge(out_taken, s)
                for h in range(DC):
                    for c in range(DC):
                        last = M(B[:, 256 * h:256 * (h + 1)], wq[:, c, h * P:(h + 1) * P],
                                 xnT[:, c, :, :].rearrange("p t n -> p (t n)"), start=(c == 0), stop=(c == DC - 1))
                last.then_inc(q_psum, 1)

            def scores(s, half, par):
                t = s + 1
                if half == 0:
                    pe.wait_ge(q_ready, half_of(t) + 1)
                if has(s, t - 1):
                    pe.wait_ge(s_ready, 2 * t - 1 + half)
                for q in range(2):
                    last = M(S[half][:, q, 0:QUART], qT[:, half, par, :],
                             kblock[:, ds(t_batch(t), 1), half, q * QUART:(q + 1) * QUART].rearrange("p a n -> p (a n)"),
                             start=True, stop=True)
                last.then_inc(s_psum, 1)

            def t_batch(t):
                return t // (TILES // BATCH)

            def transpose_scores(s, g, par):
                c0, c1 = GROUPS[g]
                if g == 0:
                    pe.wait_ge(s_ready, 2 * s + 1)
                if g == 1:
                    pe.wait_ge(s_ready, 2 * s + 2)
                if not isinstance(s, int) or s > 0 or g > 0:
                    pe.wait_ge(p_ready, 3 * s + g)
                for c in range(c0, c1):
                    last = transpose(T[:, c - c0, :], s_sb[par][:, c * P:(c + 1) * P])
                last.then_inc(t_psum, 1)

            def slot(s, par):
                if has(s, s):
                    transpose_scores(s, 0, par)
                if has(s, s - 2):
                    pe.wait_ge(uT_ready, s - 1)
                    if par == 1 and has(s, s + 1):
                        pe.wait_ge(q_ready, half_of(s - 1) + 2)
                    if after(s, 3):
                        pe.wait_ge(pos_ready, s - 2)
                    if isinstance(s, int) and s == 2:
                        pe.wait_ge(out_taken, 1)
                    M(B[:, 0:D + EXPERTS], ones[0:1, :], brow[0:1, :], start=True, stop=False)
                    for c in range(DC):
                        last = M(B[:, 0:D + EXPERTS], uT[par][:, c, :], wsr[:, c, :], start=False, stop=(c == DC - 1))
                    last.then_inc(r_psum, 1)
                if has(s, s - 1):
                    pe.wait_ge(o_ready, s)
                    if after(s, 2):
                        pe.wait_ge(uT_ready, s - 1)
                    for c in range(DC):
                        last = transpose(A[:, c, :], o_sb[1 - par][:, c * P:(c + 1) * P])
                    last.then_inc(oT_psum, 1)
                if has(s, s + 1):
                    scores(s, 0, 1 - par)
                if has(s, s):
                    transpose_scores(s, 1, par)
                if has(s, s - 1):
                    pe.wait_ge(oT_ready, s)
                    if has(s, s - 2):
                        pe.wait_ge(r_taken, s - 1)
                    elif isinstance(s, int) and s == 1:
                        pe.wait_ge(q_ready, 2)
                    for c in range(DC):
                        last = M(B[:, 0:D], oT[:, c, :], wo[:, c, :], start=(c == 0), stop=(c == DC - 1))
                    last.then_inc(out_psum, 1)
                if has(s, s + 1):
                    scores(s, 1, 1 - par)
                if has(s, s):
                    transpose_scores(s, 2, par)
                if par == 0 and has(s, s + 2) and not opening(s):
                    transpose_x(s, half_of(s) + 1)
                if has(s, s - 2):
                    pe.wait_ge(chosen_ready, s - 1)
                    if has(s, s - 1):
                        pe.wait_ge(out_taken, s)
                    else:
                        pe.wait_ge(r_taken, s - 1)
                    M(B[:, 0:EXPERTS], before16[:, :], chosen[:, :], start=True, stop=False)
                    M(B[:, 0:EXPERTS], ones16[:, :], seen[:, :], start=False, stop=True).then_inc(rank_psum, 1)
                if has(s, s):
                    if after(s, 1):
                        pe.wait_ge(o_ready, s)
                    for g, (c0, c1) in enumerate(GROUPS):
                        pe.wait_ge(p_ready, 3 * s + g + 1)
                        for c in range(c0, c1):
                            rows = P if c < CH - 1 else LASTROWS
                            last = M(O[:, HEAD0[c] * ODIM:(HEAD0[c] + SPAN) * ODIM], pT[par][0:rows, c, :],
                                     vblock[0:rows, ds(t_batch(s), 1), c, :, :].rearrange("p a h j -> p (a h j)"),
                                     start=(c == 0), stop=(c == CH - 1), skip_group_check=True)
                    last.then_inc(o_psum, 1)
                if has(s, s - 1):
                    pe.wait_ge(u_ready, s)
                    if par == 0 and has(s, s + 2):
                        pe.wait_ge(xT_ready, half_of(s) + 2)
                    else:
                        pe.wait_ge(oT_ready, s)
                    for c in range(DC):
                        last = transpose(A[:, c, :], urow[1 - par][0][:, c * P:(c + 1) * P])
                    last.then_inc(uT_psum, 1)
                if par == 0 and has(s, s + 2) and not opening(s):
                    queries(s, half_of(s) + 1)

            transpose_x(-1, 0)
            queries(-1, 0)
            pe.wait_ge(vblock_ready, BATCH)
            pe.wait_ge(arrived["wo"], 16)
            pe.wait_ge(wsr_ready, 1)
            pe.wait_ge(arrived["cent"], 16)
            pe.wait_ge(arrived["ebias"], 16)
            slots(pe, slot)
            pe.wait_ge(pos_ready, TILES)
            M(B[:, 0:EXPERTS], ones16[:, :], seen[:, :], start=True, stop=True).then_inc(count_psum, 1)

            pe.wait_ge(table_ready, 1)
            pe.wait_ge(arrived["wr"], 16)
            pe.wait_ge(s_ready, 2 * TILES)
            def list_transposes(i, j):
                pe.wait_ge(l_arrived[j], 16 * i + 16)
                for c in range(DC):
                    last = transpose(S[j % 2][:, 0, c * P:(c + 1) * P], lrow[j][:, c * P:(c + 1) * P])
                last.then_inc(uT_psum, 1)

            def list_round(i, more):
                cols = [pe.value_load(expert_i[0:1, ds(i * NB + j, 1)], min_val=0, max_val=(EXPERTS - 1) * D)
                        for j in range(NB)]
                for j in range(NB):
                    k = i * NB + j
                    if j < NB - 1:
                        list_transposes(i, j + 1)
                    elif more:
                        list_transposes(i + 1, 0)
                    pe.wait_ge(uT_ready, TILES + k + 1)
                    pe.wait_ge(out_taken, TILES + k - 1)
                    for c in range(DC):
                        last = M(S[j % 2][:, 1, 0:D], uT[j % 2][:, c, :], wr[:, c, ds(cols[j], D)],
                                 start=(c == 0), stop=(c == DC - 1))
                    last.then_inc(out_psum, 1)

            list_transposes(0, 0)
            with pe.Fori(0, LISTS // NB - 1) as i:
                list_round(i, True)
            list_round(LISTS // NB - 1, False)

    return nc


_OUTS = [((TOKENS, D), "float32")]


def kernel(x, ctx_1024, _lenS2, L0_xattn_Wq, L0_xattn_Wk, L0_xattn_Wv, L0_xattn_Wo, L0_ffn_centroids,
           L0_ffn_expert_biases, L0_ffn_Wr, L0_ffn_br, L0_ffn_Ws, L0_ffn_bs):
    import concourse.bacc as bacc
    from concourse.bass_utils import run_bass_kernel_spmd

    a = np.asarray
    laid = {
        "x": a(x).reshape(TOKENS, D),
        "ctxT": a(ctx_1024).transpose(2, 0, 1),
        "lens": a(_lenS2),
        "wq": a(L0_xattn_Wq), "wk": a(L0_xattn_Wk), "wv": a(L0_xattn_Wv), "wo": a(L0_xattn_Wo),
        "centT": a(L0_ffn_centroids).T,
        "ebias": a(L0_ffn_expert_biases),
        "wrT": a(L0_ffn_Wr).transpose(2, 0, 1).reshape(D, EXPERTS * D),
        "br": a(L0_ffn_br),
        "wsT": a(L0_ffn_Ws).transpose(2, 0, 1),
        "bs": a(L0_ffn_bs),
        "const": _constants(),
    }
    nc = bacc.Bacc("TRN2", target_bir_lowering=False, num_devices=1)
    arrays, args = {}, []
    for name, v in laid.items():
        v = np.ascontiguousarray(v)
        arrays[f"in_{name}"] = v
        args.append(nc.dram_tensor(f"in_{name}", v.shape, mybir.dt.from_np(v.dtype), kind="ExternalInput").ap())
    for i, (shape, dt) in enumerate(_OUTS):
        args.append(nc.dram_tensor(f"out_{i}", shape, mybir.dt.from_np(np.dtype(dt)), kind="ExternalOutput").ap())
    build(nc, *args)
    r = run_bass_kernel_spmd(nc, [arrays], core_ids=[0])
    return r.results[0]["out_0"].reshape(BATCH, SEQ, D)
```
